# Optimizing a Trainium2 kernel written in Bass

```python
import numpy as np
import jax
import jax.numpy as jnp

def _softmax(x, axis=-1):
    return jax.nn.softmax(x, axis=axis)

def _gelu(x):
    return jax.nn.gelu(x, approximate=True)

def _silu(x):
    return jax.nn.silu(x)

def _sigmoid(x):
    return jax.nn.sigmoid(x)

def _layernorm(x, axis=-1, eps=1e-05):
    m = jnp.mean(x, axis=axis, keepdims=True)
    v = jnp.var(x, axis=axis, keepdims=True)
    return (x - m) / jnp.sqrt(v + eps)

def _scatter_add(tgt, idx, src, axis=0):
    return tgt.at[idx].add(src)

def _segment_sum(src, seg, n):
    return jax.ops.segment_sum(src, seg, n)
kernel_name = 'mk_dlrm_tower_d1_rec_r8_2fca9b'

def setup_inputs(seed: int=0):
    np.random.seed(seed)
    _w = jnp.asarray

    def _rec_inputs():
        import jax
        import jax.numpy as jnp
        _tk = jax.random.key(seed)
        dense_ctx = jax.random.normal(jax.random.fold_in(_tk, 190), (512, 16), jnp.float32)
        ids = jnp.stack([jax.random.randint(jax.random.fold_in(_tk, 200 + f), (512,), 0, v, jnp.int32) for f, v in enumerate([12500, 1000, 1000, 1250, 12500, 12500, 12500, 1000, 12500, 1000, 1250, 1250, 1000, 1250, 1000, 1000, 12500, 1250, 12500, 1250, 12500, 1250, 1250, 1000, 1000, 1250, 1250, 1250, 1250, 1250, 1000, 1000])], axis=1)
        tbl_0 = 0.05 * jax.random.normal(jax.random.fold_in(_tk, 500 + 0), (12500, 256), jnp.float32)
        tbl_1 = 0.05 * jax.random.normal(jax.random.fold_in(_tk, 500 + 1), (1000, 256), jnp.float32)
        tbl_2 = 0.05 * jax.random.normal(jax.random.fold_in(_tk, 500 + 2), (1000, 256), jnp.float32)
        tbl_3 = 0.05 * jax.random.normal(jax.random.fold_in(_tk, 500 + 3), (1250, 256), jnp.float32)
        tbl_4 = 0.05 * jax.random.normal(jax.random.fold_in(_tk, 500 + 4), (12500, 256), jnp.float32)
        tbl_5 = 0.05 * jax.random.normal(jax.random.fold_in(_tk, 500 + 5), (12500, 256), jnp.float32)
        tbl_6 = 0.05 * jax.random.normal(jax.random.fold_in(_tk, 500 + 6), (12500, 256), jnp.float32)
        tbl_7 = 0.05 * jax.random.normal(jax.random.fold_in(_tk, 500 + 7), (1000, 256), jnp.float32)
        tbl_8 = 0.05 * jax.random.normal(jax.random.fold_in(_tk, 500 + 8), (12500, 256), jnp.float32)
        tbl_9 = 0.05 * jax.random.normal(jax.random.fold_in(_tk, 500 + 9), (1000, 256), jnp.float32)
        tbl_10 = 0.05 * jax.random.normal(jax.random.fold_in(_tk, 500 + 10), (1250, 256), jnp.float32)
        tbl_11 = 0.05 * jax.random.normal(jax.random.fold_in(_tk, 500 + 11), (1250, 256), jnp.float32)
        tbl_12 = 0.05 * jax.random.normal(jax.random.fold_in(_tk, 500 + 12), (1000, 256), jnp.float32)
        tbl_13 = 0.05 * jax.random.normal(jax.random.fold_in(_tk, 500 + 13), (1250, 256), jnp.float32)
        tbl_14 = 0.05 * jax.random.normal(jax.random.fold_in(_tk, 500 + 14), (1000, 256), jnp.float32)
        tbl_15 = 0.05 * jax.random.normal(jax.random.fold_in(_tk, 500 + 15), (1000, 256), jnp.float32)
        tbl_16 = 0.05 * jax.random.normal(jax.random.fold_in(_tk, 500 + 16), (12500, 256), jnp.float32)
        tbl_17 = 0.05 * jax.random.normal(jax.random.fold_in(_tk, 500 + 17), (1250, 256), jnp.float32)
        tbl_18 = 0.05 * jax.random.normal(jax.random.fold_in(_tk, 500 + 18), (12500, 256), jnp.float32)
        tbl_19 = 0.05 * jax.random.normal(jax.random.fold_in(_tk, 500 + 19), (1250, 256), jnp.float32)
        tbl_20 = 0.05 * jax.random.normal(jax.random.fold_in(_tk, 500 + 20), (12500, 256), jnp.float32)
        tbl_21 = 0.05 * jax.random.normal(jax.random.fold_in(_tk, 500 + 21), (1250, 256), jnp.float32)
        tbl_22 = 0.05 * jax.random.normal(jax.random.fold_in(_tk, 500 + 22), (1250, 256), jnp.float32)
        tbl_23 = 0.05 * jax.random.normal(jax.random.fold_in(_tk, 500 + 23), (1000, 256), jnp.float32)
        tbl_24 = 0.05 * jax.random.normal(jax.random.fold_in(_tk, 500 + 24), (1000, 256), jnp.float32)
        tbl_25 = 0.05 * jax.random.normal(jax.random.fold_in(_tk, 500 + 25), (1250, 256), jnp.float32)
        tbl_26 = 0.05 * jax.random.normal(jax.random.fold_in(_tk, 500 + 26), (1250, 256), jnp.float32)
        tbl_27 = 0.05 * jax.random.normal(jax.random.fold_in(_tk, 500 + 27), (1250, 256), jnp.float32)
        tbl_28 = 0.05 * jax.random.normal(jax.random.fold_in(_tk, 500 + 28), (1250, 256), jnp.float32)
        tbl_29 = 0.05 * jax.random.normal(jax.random.fold_in(_tk, 500 + 29), (1250, 256), jnp.float32)
        tbl_30 = 0.05 * jax.random.normal(jax.random.fold_in(_tk, 500 + 30), (1000, 256), jnp.float32)
        tbl_31 = 0.05 * jax.random.normal(jax.random.fold_in(_tk, 500 + 31), (1000, 256), jnp.float32)
        _rk = jax.random.fold_in(_tk, 7)
        W_top1 = 0.0441942 * jax.random.normal(jax.random.fold_in(_tk, 801), (512, 512), jnp.float32)
        W_top2 = 0.0441942 * jax.random.normal(jax.random.fold_in(_tk, 802), (512, 256), jnp.float32)
        W_top3 = 0.0625 * jax.random.normal(jax.random.fold_in(_tk, 803), (256, 1), jnp.float32)
        b_top1 = jnp.zeros((512,), jnp.float32)
        b_top2 = jnp.zeros((256,), jnp.float32)
        return (dense_ctx, ids, tbl_0, tbl_1, tbl_2, tbl_3, tbl_4, tbl_5, tbl_6, tbl_7, tbl_8, tbl_9, tbl_10, tbl_11, tbl_12, tbl_13, tbl_14, tbl_15, tbl_16, tbl_17, tbl_18, tbl_19, tbl_20, tbl_21, tbl_22, tbl_23, tbl_24, tbl_25, tbl_26, tbl_27, tbl_28, tbl_29, tbl_30, tbl_31, W_top1, b_top1, W_top2, b_top2, W_top3)
    dense_ctx, ids, tbl_0, tbl_1, tbl_2, tbl_3, tbl_4, tbl_5, tbl_6, tbl_7, tbl_8, tbl_9, tbl_10, tbl_11, tbl_12, tbl_13, tbl_14, tbl_15, tbl_16, tbl_17, tbl_18, tbl_19, tbl_20, tbl_21, tbl_22, tbl_23, tbl_24, tbl_25, tbl_26, tbl_27, tbl_28, tbl_29, tbl_30, tbl_31, W_top1, b_top1, W_top2, b_top2, W_top3 = _rec_inputs()

    def _L0_rec_setup():
        import jax, jax.numpy as jnp
        import numpy as np
        B, N, D = (1024, 32, 256)
        key = jax.random.key(seed)
        x = jax.random.normal(key, (B, N, D), dtype=jnp.float32)
        return {'x': x}
    _L0_rec_all = _L0_rec_setup()
    _L0_rec_in = {k: v for k, v in _L0_rec_all.items() if k in ()}
    del _L0_rec_all
    return {'dense_ctx': dense_ctx, 'ids': ids, 'tbl_0': tbl_0, 'tbl_1': tbl_1, 'tbl_2': tbl_2, 'tbl_3': tbl_3, 'tbl_4': tbl_4, 'tbl_5': tbl_5, 'tbl_6': tbl_6, 'tbl_7': tbl_7, 'tbl_8': tbl_8, 'tbl_9': tbl_9, 'tbl_10': tbl_10, 'tbl_11': tbl_11, 'tbl_12': tbl_12, 'tbl_13': tbl_13, 'tbl_14': tbl_14, 'tbl_15': tbl_15, 'tbl_16': tbl_16, 'tbl_17': tbl_17, 'tbl_18': tbl_18, 'tbl_19': tbl_19, 'tbl_20': tbl_20, 'tbl_21': tbl_21, 'tbl_22': tbl_22, 'tbl_23': tbl_23, 'tbl_24': tbl_24, 'tbl_25': tbl_25, 'tbl_26': tbl_26, 'tbl_27': tbl_27, 'tbl_28': tbl_28, 'tbl_29': tbl_29, 'tbl_30': tbl_30, 'tbl_31': tbl_31, 'W_top1': W_top1, 'b_top1': b_top1, 'W_top2': W_top2, 'b_top2': b_top2, 'W_top3': W_top3}

def reference(dense_ctx, ids, tbl_0, tbl_1, tbl_2, tbl_3, tbl_4, tbl_5, tbl_6, tbl_7, tbl_8, tbl_9, tbl_10, tbl_11, tbl_12, tbl_13, tbl_14, tbl_15, tbl_16, tbl_17, tbl_18, tbl_19, tbl_20, tbl_21, tbl_22, tbl_23, tbl_24, tbl_25, tbl_26, tbl_27, tbl_28, tbl_29, tbl_30, tbl_31, W_top1, b_top1, W_top2, b_top2, W_top3):
    import jax
    import jax.numpy as jnp

    def _L0_rec_ref(x):
        import jax, jax.numpy as jnp
        import numpy as np
        B, N, D = (1024, 32, 256)
        'Second-order feature interaction (DLRM dot interaction).\n\n            Computes dot(x_i, x_j) for all field pairs i < j (self_interaction=False),\n            flattened in row-major upper-triangular order -> [B, N*(N-1)/2].\n            Matches tf.boolean_mask(dot_products, strictly_upper_mask) ordering.\n            '
        b, n, d = x.shape
        iu, ju = jnp.triu_indices(n, k=1)
        dots = jnp.einsum('bnd,bmd->bnm', x, x)
        return dots[:, iu, ju]
    e = jnp.stack([tbl_0[ids[:, 0]], tbl_1[ids[:, 1]], tbl_2[ids[:, 2]], tbl_3[ids[:, 3]], tbl_4[ids[:, 4]], tbl_5[ids[:, 5]], tbl_6[ids[:, 6]], tbl_7[ids[:, 7]], tbl_8[ids[:, 8]], tbl_9[ids[:, 9]], tbl_10[ids[:, 10]], tbl_11[ids[:, 11]], tbl_12[ids[:, 12]], tbl_13[ids[:, 13]], tbl_14[ids[:, 14]], tbl_15[ids[:, 15]], tbl_16[ids[:, 16]], tbl_17[ids[:, 17]], tbl_18[ids[:, 18]], tbl_19[ids[:, 19]], tbl_20[ids[:, 20]], tbl_21[ids[:, 21]], tbl_22[ids[:, 22]], tbl_23[ids[:, 23]], tbl_24[ids[:, 24]], tbl_25[ids[:, 25]], tbl_26[ids[:, 26]], tbl_27[ids[:, 27]], tbl_28[ids[:, 28]], tbl_29[ids[:, 29]], tbl_30[ids[:, 30]], tbl_31[ids[:, 31]]], axis=1)
    z = _L0_rec_ref(e)
    z = z.reshape(z.shape[0], -1)
    h = jnp.concatenate([z, dense_ctx], axis=1)
    h = jnp.maximum(h @ W_top1 + b_top1, 0.0)
    h = jnp.maximum(h @ W_top2 + b_top2, 0.0)
    y = h @ W_top3
    return y

_drawn_inputs = setup_inputs


def setup_inputs(seed=0):
    import zlib

    import numpy as np

    out = dict(_drawn_inputs(seed))
    spreads = {'b_top1': (0.0, 0.1), 'b_top2': (0.0, 0.1)}
    factors = {}
    for name, (base, spread) in spreads.items():
        noise = np.random.default_rng([zlib.crc32(name.encode()), seed]).standard_normal(out[name].shape)
        drawn = base * np.exp(spread * noise) if base else spread * noise
        out[name] = jnp.asarray(drawn.astype(out[name].dtype))
    for name, factor in factors.items():
        out[name] = (out[name] * factor).astype(out[name].dtype)
    return out
```

```python
from contextlib import ExitStack

import concourse.bass as bass
from concourse import mybir

F32 = mybir.dt.float32
I32 = mybir.dt.int32
ALU = mybir.AluOpType
ACT = mybir.ActivationFunctionType

P = 128
FIELDS = 32
QUADS = P // FIELDS
BATCH = 512
DIM = 256
CHUNKS = DIM // P
GROUPS = BATCH // QUADS
STEP = 16
PAIRS = STEP // 2
HALF = STEP // 2
STEPS = GROUPS // STEP
BLOCK_STEPS = 2
BLOCK = BLOCK_STEPS * STEP * QUADS
LOOPED_BLOCKS = STEPS // BLOCK_STEPS - 1
SMALL = STEP * QUADS
SLOTS = FIELDS // QUADS
H1 = 512
H2 = 256
N1 = H1 // P
N2 = H2 // P
DENSE = 16


def tower_kernel(nc, ids, row_base, tables, dense, w1, w2, vectors, y):
    with ExitStack() as ctx:
        def sb(name, shape, dt=F32):
            return ctx.enter_context(nc.sbuf_tensor(name, shape, dt))

        def psum(name, shape):
            return ctx.enter_context(nc.psum_tensor(name, shape, F32))

        def sem(name):
            return ctx.enter_context(nc.semaphore(name))

        ids_in = sb("ids_in", [P, P], I32)
        ids_t = sb("ids_t", [P, P], I32)
        base_sb = sb("base_sb", [P, 1], I32)
        idx = sb("idx", [P, GROUPS], I32)
        ident = sb("ident", [P, P])
        rows = sb("rows", [P, STEP, DIM])
        xt = sb("xt", [P, 2, 2, DIM])
        z = sb("z", [P, SLOTS, BATCH])
        dense_in = sb("dense_in", [P, P])
        dense_t = sb("dense_t", [P, P])
        w1_sb = sb("w1_sb", [P, SLOTS, H1])
        w2_sb = sb("w2_sb", [P, N1, H2])
        vec_sb = sb("vec_sb", [P, N1 + 2 * N2])
        h1 = sb("h1", [P, N1, BLOCK])
        h2 = sb("h2", [P, N2, BLOCK])
        y_row = sb("y_row", [1, BATCH])
        b1 = vec_sb[:, 0:N1]
        b2 = vec_sb[:, N1:N1 + N2]
        w3 = vec_sb[:, N1 + N2:N1 + 2 * N2]

        xt_ps = psum("xt_ps", [P, 2, 2, DIM])
        gram_ps = psum("gram_ps", [P, 2, HALF, P])
        mlp_ps = psum("mlp_ps", [P, 2, 4, BLOCK])
        y_ps = mlp_ps[0:1, 0, 3, :]

        ids_loaded = sem("ids_loaded")
        base_loaded = sem("base_loaded")
        dense_loaded = sem("dense_loaded")
        w1_loaded = sem("w1_loaded")
        w2_loaded = sem("w2_loaded")
        vec_loaded = sem("vec_loaded")
        ids_turned = sem("ids_turned")
        idx_ready = sem("idx_ready")
        ident_zeroed = sem("ident_zeroed")
        ident_ready = sem("ident_ready")
        dense_turned = sem("dense_turned")
        dense_ready = sem("dense_ready")
        rows_landed = [sem(f"rows_landed_{n}") for n in range(STEP)]
        transposed = sem("transposed")
        xt_dve = sem("xt_dve")
        xt_act = sem("xt_act")
        gram_done = sem("gram_done")
        z_dve = sem("z_dve")
        z_act = sem("z_act")
        h1_done = sem("h1_done")
        h1_act = sem("h1_act")
        h1_dve = sem("h1_dve")
        h2_done = sem("h2_done")
        h2_act = sem("h2_act")
        h2_dve = sem("h2_dve")
        y_done = sem("y_done")
        y_copied = sem("y_copied")
        y_stored = sem("y_stored")

        z_by_quad = z[:].rearrange("p s (g q) -> p q g s", q=QUADS)
        y_by_column = y_row[:].rearrange("o (q r c) -> o c r q", q=QUADS, c=4)

        def copy_dots(copy, quads, first, slot0, count):
            half, at = slot0 // HALF, slot0 % HALF
            for q in quads:
                for jq in range(QUADS):
                    lo = 1 if jq == 0 else 0
                    j0 = FIELDS * q + SLOTS * jq
                    last = copy(
                        z_by_quad[FIELDS * jq:FIELDS * (jq + 1), q, bass.ds(first, count), lo:SLOTS],
                        gram_ps[FIELDS * q:FIELDS * (q + 1), half, at:at + count, j0 + lo:j0 + SLOTS])
            return last

        block = ctx.enter_context(nc.Block())

        @block.sync
        def _(sp):
            sp.dma_start(ids_in[:], ids.rearrange("(p c) f -> p (c f)", c=4)).then_inc(ids_loaded, 16)
            sp.dma_start(dense_in[:], dense.rearrange("(p c) f -> p (c f)", c=4)).then_inc(dense_loaded, 16)
            sp.dma_start(w1_sb[:], w1).then_inc(w1_loaded, 16)
            sp.dma_start(w2_sb[:], w2.rearrange("(k p) n -> p k n", p=P)).then_inc(w2_loaded, 16)
            sp.wait_ge(y_copied, LOOPED_BLOCKS + 2)
            sp.dma_start(y.rearrange("b o -> o b"), y_row[:]).then_inc(y_stored, 16)
            sp.wait_ge(y_stored, 16)

        @block.gpsimd
        def _(pool):
            nc.gpsimd.memset(ident[:], 0.0).then_inc(ident_zeroed, 1)
            pool.wait_ge(ident_zeroed, 1)
            nc.gpsimd.affine_select(out=ident[:], in_=ident[:], compare_op=ALU.not_equal, fill=1.0,
                                    base=0, pattern=[[-1, P]], channel_multiplier=1).then_inc(ident_ready, 1)
            pool.wait_ge(idx_ready, 1)
            for g in range(GROUPS):
                if g >= STEP:
                    pool.wait_ge(transposed, g - STEP + 1)
                pool.indirect_dma_start(rows[:, g % STEP, :], None, tables,
                                        bass.IndirectOffsetOnAxis(idx[:, g:g + 1], 0)
                                        ).then_inc(rows_landed[g % STEP], 16)

        @block.tensor
        def _(pe):
            def transpose_pair(s, p):
                for n in (2 * p, 2 * p + 1):
                    pe.wait_ge(rows_landed[n], 16 * (s + 1))
                    for k in range(CHUNKS):
                        last = nc.tensor.transpose(xt_ps[:, p % 2, n % 2, P * k:P * (k + 1)],
                                                   rows[:, n, P * k:P * (k + 1)], ident[:])
                    last.then_inc(transposed, 1)

            def gram_pair(s, p):
                if p % (HALF // 2) == 0:
                    pe.wait_ge(z_dve, 2 * s + 2 * p // HALF + 1)
                    pe.wait_ge(z_act, 2 * s + 2 * p // HALF + 1)
                pe.wait_ge(xt_act if p % 2 else xt_dve, PAIRS // 2 * s + p // 2 + 1)
                for n in range(2):
                    slot = 2 * p + n
                    for k in range(CHUNKS):
                        x = xt[:, p % 2, n, P * k:P * (k + 1)]
                        last = nc.tensor.matmul(gram_ps[:, slot // HALF, slot % HALF, :], x, x,
                                                start=(k == 0), stop=(k == CHUNKS - 1))
                last.then_inc(gram_done, 1)

            def step(s, middle=None):
                transpose_pair(s, 0)
                for p in range(1, PAIRS):
                    transpose_pair(s, p)
                    gram_pair(s, p - 1)
                    if middle and p == PAIRS // 2:
                        middle()
                gram_pair(s, PAIRS - 1)

            def mlp(b, col, n, halves):
                pe.wait_ge(z_dve, 2 + halves)
                pe.wait_ge(z_act, 2 + halves)
                pe.wait_ge(y_copied, b)
                for m in range(N1):
                    for s in range(SLOTS):
                        last = nc.tensor.matmul(mlp_ps[:, m // 2, m % 2, 0:n],
                                                w1_sb[:, s, P * m:P * (m + 1)],
                                                z[:, s, bass.ds(col, n)],
                                                start=(s == 0), stop=(s == SLOTS - 1))
                    if m % 2:
                        last.then_inc(h1_done, 1)
                for m in range(N2):
                    for k in range(N1):
                        if m == 0 and k % 2 == 0:
                            pe.wait_ge(h1_dve if k else h1_act, b + 1)
                        last = nc.tensor.matmul(mlp_ps[:, m, 2, 0:n], w2_sb[:, k, P * m:P * (m + 1)],
                                                h1[:, k, 0:n], start=(k == 0), stop=(k == N1 - 1))
                    last.then_inc(h2_done, 1)
                for m in range(N2):
                    pe.wait_ge(h2_dve if m else h2_act, b + 1)
                    last = nc.tensor.matmul(y_ps[:, 0:n], w3[:, m:m + 1], h2[:, m, 0:n],
                                            start=(m == 0), stop=(m == N2 - 1))
                last.then_inc(y_done, 1)

            pe.wait_ge(ident_ready, 1)
            pe.wait_ge(dense_ready, 1)
            pe.wait_ge(w1_loaded, 16)
            pe.wait_ge(w2_loaded, 16)
            pe.wait_ge(vec_loaded, 16)
            with pe.Fori(0, LOOPED_BLOCKS) as b:
                with pe.Fori(0, BLOCK_STEPS) as t:
                    step(BLOCK_STEPS * b + t)
                mlp(b, BLOCK * b, BLOCK, 2 * BLOCK_STEPS * b + 2 * BLOCK_STEPS)
            step(STEPS - 2)
            step(STEPS - 1, lambda: mlp(LOOPED_BLOCKS, BATCH - 2 * SMALL, SMALL, 2 * STEPS - 2))
            mlp(LOOPED_BLOCKS + 1, BATCH - SMALL, SMALL, 2 * STEPS)

        @block.vector
        def _(dve):
            dve.wait_ge(ids_loaded, 16)
            nc.vector.transpose(ids_t[:], ids_in[:]).then_inc(ids_turned, 1)
            dve.wait_ge(ids_turned, 1)
            dve.wait_ge(base_loaded, 16)
            nc.vector.tensor_tensor(idx[:], ids_t[:], base_sb[:, 0:1].to_broadcast([P, GROUPS]),
                                    ALU.add).then_inc(idx_ready, 1)
            dve.sem_inc(z_dve, 2)
            dve.wait_ge(dense_loaded, 16)
            nc.vector.transpose(dense_t[:], dense_in[:]).then_inc(dense_turned, 1)
            dve.wait_ge(dense_turned, 1)
            for q in range(QUADS):
                last = nc.vector.tensor_copy(z_by_quad[0:FIELDS, q, :, 0],
                                             dense_t[FIELDS * q:FIELDS * (q + 1), :])
            last.then_inc(dense_ready, 1)

            def copy_pair(s, p):
                dve.wait_ge(transposed, STEP * s + 2 * p + 2)
                nc.vector.tensor_copy(xt[:, 0], xt_ps[:, 0]).then_inc(xt_dve, 1)

            def dots(s, slot0, count):
                dve.wait_ge(gram_done, PAIRS * s + (slot0 + count) // 2)
                return copy_dots(nc.vector.tensor_copy, (0, 1), STEP * s + slot0, slot0, count)

            def step(s, middle=None):
                for p in range(0, PAIRS, 2):
                    copy_pair(s, p)
                    if p == PAIRS // 2:
                        dots(s, 0, HALF).then_inc(z_dve, 1)
                        if middle:
                            middle()
                if middle:
                    dots(s, HALF, HALF // 2)
                    dots(s, HALF + HALF // 2, HALF // 2).then_inc(z_dve, 1)
                else:
                    dots(s, HALF, HALF).then_inc(z_dve, 1)

            def mlp(b, c, r0, n):
                dve.wait_ge(h1_done, 2 * b + 2)
                for m in (2, 3):
                    last = nc.vector.tensor_scalar(h1[:, m, 0:n], mlp_ps[:, 1, m % 2, 0:n],
                                                   b1[:, m:m + 1], 0.0, ALU.add, ALU.max)
                last.then_inc(h1_dve, 1)
                dve.wait_ge(h2_done, 2 * b + 2)
                nc.vector.tensor_scalar(h2[:, 1, 0:n], mlp_ps[:, 1, 2, 0:n], b2[:, 1:2], 0.0,
                                        ALU.add, ALU.max).then_inc(h2_dve, 1)
                dve.wait_ge(y_done, b + 1)
                nc.vector.tensor_copy(
                    y_by_column[:, bass.ds(c, 1), r0:r0 + n // QUADS, :],
                    y_ps[:, 0:n].rearrange("o (c r q) -> o c r q", c=1, q=QUADS)).then_inc(y_copied, 1)

            dve.wait_ge(vec_loaded, 16)
            with dve.Fori(0, LOOPED_BLOCKS) as b:
                with dve.Fori(0, BLOCK_STEPS) as t:
                    step(BLOCK_STEPS * b + t)
                mlp(b, b, 0, BLOCK)
            step(STEPS - 2)
            step(STEPS - 1, lambda: mlp(LOOPED_BLOCKS, LOOPED_BLOCKS, 0, SMALL))
            mlp(LOOPED_BLOCKS + 1, LOOPED_BLOCKS, SMALL // QUADS, SMALL)

        @block.scalar
        def _(act):
            act.dma_start(base_sb[:], row_base).then_inc(base_loaded, 16)
            act.dma_start(vec_sb[:], vectors).then_inc(vec_loaded, 16)
            act.sem_inc(z_act, 2)

            def copy_pair(s, p):
                act.wait_ge(transposed, STEP * s + 2 * p + 2)
                nc.scalar.copy(xt[:, 1], xt_ps[:, 1]).then_inc(xt_act, 1)

            def dots(s, slot0, count):
                act.wait_ge(gram_done, PAIRS * s + (slot0 + count) // 2)
                return copy_dots(nc.scalar.copy, (2, 3), STEP * s + slot0, slot0, count)

            def step(s, middle=None):
                for p in range(1, PAIRS, 2):
                    copy_pair(s, p)
                    if p == PAIRS // 2 - 1:
                        dots(s, 0, HALF).then_inc(z_act, 1)
                        if middle:
                            middle()
                if middle:
                    dots(s, HALF, HALF // 2)
                    dots(s, HALF + HALF // 2, HALF // 2).then_inc(z_act, 1)
                else:
                    dots(s, HALF, HALF).then_inc(z_act, 1)

            def mlp(b, n):
                act.wait_ge(h1_done, 2 * b + 1)
                for m in (0, 1):
                    last = nc.scalar.activation(h1[:, m, 0:n], mlp_ps[:, 0, m, 0:n], ACT.Relu,
                                                bias=b1[:, m:m + 1])
                last.then_inc(h1_act, 1)
                act.wait_ge(h2_done, 2 * b + 1)
                nc.scalar.activation(h2[:, 0, 0:n], mlp_ps[:, 0, 2, 0:n], ACT.Relu,
                                     bias=b2[:, 0:1]).then_inc(h2_act, 1)

            act.wait_ge(vec_loaded, 16)
            with act.Fori(0, LOOPED_BLOCKS) as b:
                with act.Fori(0, BLOCK_STEPS) as t:
                    step(BLOCK_STEPS * b + t)
                mlp(b, BLOCK)
            step(STEPS - 2)
            step(STEPS - 1, lambda: mlp(LOOPED_BLOCKS, SMALL))
            mlp(LOOPED_BLOCKS + 1, SMALL)


def interaction_weights(w_top1):
    import numpy as np

    out = np.zeros((QUADS, FIELDS, SLOTS, w_top1.shape[1]), w_top1.dtype)
    i, j = np.triu_indices(FIELDS, k=1)
    out[j // SLOTS, i, j % SLOTS] = w_top1[:len(i)]
    out[0, :DENSE, 0] = w_top1[len(i):]
    return out.reshape(P, SLOTS, -1)


def kernel(**inputs):
    import numpy as np
    import concourse.bacc as bacc
    from concourse.bass_utils import run_bass_kernel_spmd

    a = {name: np.asarray(x) for name, x in inputs.items()}
    tables = [a[f"tbl_{f}"] for f in range(FIELDS)]
    starts = np.cumsum([0] + [len(t) for t in tables[:-1]]).astype(np.int32)
    dense = np.zeros((BATCH, FIELDS), a["dense_ctx"].dtype)
    dense[:, :DENSE] = a["dense_ctx"]
    arrays = {
        "ids": np.ascontiguousarray(a["ids"]),
        "row_base": np.tile(starts, QUADS).reshape(P, 1),
        "tables": np.concatenate(tables, axis=0),
        "dense": dense,
        "w1": interaction_weights(a["W_top1"]),
        "w2": np.ascontiguousarray(a["W_top2"]),
        "vectors": np.ascontiguousarray(np.concatenate(
            [a[n].reshape(-1, P) for n in ("b_top1", "b_top2", "W_top3")], axis=0).T),
    }
    nc = bacc.Bacc("TRN2", target_bir_lowering=False, num_devices=1)
    args = [nc.dram_tensor(name, x.shape, mybir.dt.from_np(x.dtype), kind="ExternalInput").ap()
            for name, x in arrays.items()]
    y = nc.dram_tensor("y", (BATCH, 1), F32, kind="ExternalOutput").ap()
    tower_kernel(nc, *args, y)
    run = run_bass_kernel_spmd(nc, [arrays], core_ids=[0])
    return run.results[0]["y"]
```

```python
from contextlib import ExitStack

import concourse.bass as bass
from concourse import mybir

F32 = mybir.dt.float32
I32 = mybir.dt.int32
ALU = mybir.AluOpType
ACT = mybir.ActivationFunctionType

P = 128
FIELDS = 32
QUADS = P // FIELDS
BATCH = 512
DIM = 256
CHUNKS = DIM // P
GROUPS = BATCH // QUADS
STEP = 16
PAIRS = STEP // 2
HALF = STEP // 2
STEPS = GROUPS // STEP
BLOCK_STEPS = 2
BLOCK = BLOCK_STEPS * STEP * QUADS
BLOCKS = BATCH // BLOCK
SLOTS = FIELDS // QUADS
H1 = 512
H2 = 256
N1 = H1 // P
N2 = H2 // P
DENSE = 16


def tower_kernel(nc, ids, row_base, tables, dense, w1, w2, vectors, y):
    with ExitStack() as ctx:
        def sb(name, shape, dt=F32):
            return ctx.enter_context(nc.sbuf_tensor(name, shape, dt))

        def psum(name, shape):
            return ctx.enter_context(nc.psum_tensor(name, shape, F32))

        def sem(name):
            return ctx.enter_context(nc.semaphore(name))

        ids_in = sb("ids_in", [P, P], I32)
        ids_t = sb("ids_t", [P, P], I32)
        base_sb = sb("base_sb", [P, 1], I32)
        idx = sb("idx", [P, GROUPS], I32)
        ident = sb("ident", [P, P])
        rows = sb("rows", [P, STEP, DIM])
        xt = sb("xt", [P, 2, 2, DIM])
        z = sb("z", [P, SLOTS, BATCH])
        dense_in = sb("dense_in", [P, P])
        dense_t = sb("dense_t", [P, P])
        w1_sb = sb("w1_sb", [P, SLOTS, H1])
        w2_sb = sb("w2_sb", [P, N1, H2])
        vec_sb = sb("vec_sb", [P, N1 + 2 * N2])
        h1 = sb("h1", [P, N1, BLOCK])
        h2 = sb("h2", [P, N2, BLOCK])
        y_row = sb("y_row", [1, BATCH])
        b1 = vec_sb[:, 0:N1]
        b2 = vec_sb[:, N1:N1 + N2]
        w3 = vec_sb[:, N1 + N2:N1 + 2 * N2]

        xt_ps = psum("xt_ps", [P, 2, 2, DIM])
        gram_ps = psum("gram_ps", [P, 2, HALF, P])
        mlp_ps = psum("mlp_ps", [P, 2, 4, BLOCK])
        y_ps = mlp_ps[0:1, 0, 3, :]

        ids_loaded = sem("ids_loaded")
        base_loaded = sem("base_loaded")
        dense_loaded = sem("dense_loaded")
        w1_loaded = sem("w1_loaded")
        w2_loaded = sem("w2_loaded")
        vec_loaded = sem("vec_loaded")
        ids_turned = sem("ids_turned")
        idx_ready = sem("idx_ready")
        ident_zeroed = sem("ident_zeroed")
        ident_ready = sem("ident_ready")
        dense_turned = sem("dense_turned")
        dense_ready = sem("dense_ready")
        rows_landed = [sem(f"rows_landed_{n}") for n in range(STEP)]
        transposed = sem("transposed")
        xt_dve = sem("xt_dve")
        xt_act = sem("xt_act")
        gram_done = sem("gram_done")
        z_dve = sem("z_dve")
        z_act = sem("z_act")
        h1_done = sem("h1_done")
        h1_act = sem("h1_act")
        h1_dve = sem("h1_dve")
        h2_done = sem("h2_done")
        h2_act = sem("h2_act")
        h2_dve = sem("h2_dve")
        y_done = sem("y_done")
        y_free = sem("y_free")
        y_stored = sem("y_stored")

        z_by_quad = z[:].rearrange("p s (g q) -> p q g s", q=QUADS)
        y_by_column = y_row[:].rearrange("o (q r c) -> o c r q", q=QUADS, c=4)

        def copy_dots(copy, quads, first, slot0, count):
            half, at = slot0 // HALF, slot0 % HALF
            for q in quads:
                for jq in range(QUADS):
                    lo = 1 if jq == 0 else 0
                    j0 = FIELDS * q + SLOTS * jq
                    last = copy(
                        z_by_quad[FIELDS * jq:FIELDS * (jq + 1), q, bass.ds(first, count), lo:SLOTS],
                        gram_ps[FIELDS * q:FIELDS * (q + 1), half, at:at + count, j0 + lo:j0 + SLOTS])
            return last

        block = ctx.enter_context(nc.Block())

        @block.sync
        def _(sp):
            sp.dma_start(ids_in[:], ids.rearrange("(p c) f -> p (c f)", c=4)).then_inc(ids_loaded, 16)
            sp.wait_ge(transposed, 2)
            sp.dma_start(dense_in[:], dense.rearrange("(p c) f -> p (c f)", c=4)).then_inc(dense_loaded, 16)
            for n in range(SLOTS):
                sp.wait_ge(transposed, 2 * n + 4)
                sp.dma_start(w1_sb[:, n, :], w1[:, n, :]).then_inc(w1_loaded, 16)
            sp.wait_ge(transposed, 2 * SLOTS + 4)
            sp.dma_start(w2_sb[:], w2.rearrange("(k p) n -> p k n", p=P)).then_inc(w2_loaded, 16)
            sp.wait_ge(y_free, 1 + BLOCKS)
            sp.dma_start(y.rearrange("b o -> o b"), y_row[:]).then_inc(y_stored, 16)
            sp.wait_ge(y_stored, 16)

        @block.gpsimd
        def _(pool):
            nc.gpsimd.memset(ident[:], 0.0).then_inc(ident_zeroed, 1)
            pool.wait_ge(ident_zeroed, 1)
            nc.gpsimd.affine_select(out=ident[:], in_=ident[:], compare_op=ALU.not_equal, fill=1.0,
                                    base=0, pattern=[[-1, P]], channel_multiplier=1).then_inc(ident_ready, 1)
            pool.wait_ge(idx_ready, 1)
            for g in range(GROUPS):
                if g >= STEP:
                    pool.wait_ge(transposed, g - STEP + 1)
                pool.indirect_dma_start(rows[:, g % STEP, :], None, tables,
                                        bass.IndirectOffsetOnAxis(idx[:, g:g + 1], 0)
                                        ).then_inc(rows_landed[g % STEP], 16)

        @block.tensor
        def _(pe):
            def transpose_pair(s, p):
                for n in (2 * p, 2 * p + 1):
                    pe.wait_ge(rows_landed[n], 16 * (s + 1))
                    for k in range(CHUNKS):
                        last = nc.tensor.transpose(xt_ps[:, p % 2, n % 2, P * k:P * (k + 1)],
                                                   rows[:, n, P * k:P * (k + 1)], ident[:])
                    last.then_inc(transposed, 1)

            def gram_pair(s, p):
                if p % (HALF // 2) == 0:
                    pe.wait_ge(z_dve, 2 * s + 2 * p // HALF + 1)
                    pe.wait_ge(z_act, 2 * s + 2 * p // HALF + 1)
                pe.wait_ge(xt_act if p % 2 else xt_dve, PAIRS // 2 * s + p // 2 + 1)
                for n in range(2):
                    slot = 2 * p + n
                    for k in range(CHUNKS):
                        x = xt[:, p % 2, n, P * k:P * (k + 1)]
                        last = nc.tensor.matmul(gram_ps[:, slot // HALF, slot % HALF, :], x, x,
                                                start=(k == 0), stop=(k == CHUNKS - 1))
                last.then_inc(gram_done, 1)

            def step(s, mlp=None):
                transpose_pair(s, 0)
                for p in range(1, PAIRS):
                    transpose_pair(s, p)
                    gram_pair(s, p - 1)
                    if mlp and p in mlp:
                        mlp[p]()
                gram_pair(s, PAIRS - 1)

            def h1_half(col, half):
                for m in (2 * half, 2 * half + 1):
                    for s in range(SLOTS):
                        last = nc.tensor.matmul(mlp_ps[:, half, m % 2, :],
                                                w1_sb[:, s, P * m:P * (m + 1)],
                                                z[:, s, bass.ds(col, BLOCK)],
                                                start=(s == 0), stop=(s == SLOTS - 1))
                last.then_inc(h1_done, 1)

            def h2_all(b):
                for m in range(N2):
                    for k in range(N1):
                        if m == 0 and k % 2 == 0:
                            pe.wait_ge(h1_dve if k else h1_act, b + 1)
                        last = nc.tensor.matmul(mlp_ps[:, m, 2, :], w2_sb[:, k, P * m:P * (m + 1)],
                                                h1[:, k, :], start=(k == 0), stop=(k == N1 - 1))
                    last.then_inc(h2_done, 1)

            def y_all(b):
                for m in range(N2):
                    pe.wait_ge(h2_dve if m else h2_act, b + 1)
                    last = nc.tensor.matmul(y_ps[:, :], w3[:, m:m + 1], h2[:, m, :],
                                            start=(m == 0), stop=(m == N2 - 1))
                last.then_inc(y_done, 1)

            def mlp_stages(b, col, halves):
                def first():
                    pe.wait_ge(dense_ready, 1)
                    pe.wait_ge(w1_loaded, 16 * SLOTS)
                    pe.wait_ge(w2_loaded, 16)
                    pe.wait_ge(vec_loaded, 16)
                    pe.wait_ge(z_dve, 2 + halves)
                    pe.wait_ge(z_act, 2 + halves)
                    pe.wait_ge(y_free, b + 1)
                    h1_half(col, 0)

                return {3: first, 4: lambda: h1_half(col, 1),
                        6: lambda: h2_all(b), 7: lambda: y_all(b)}

            pe.wait_ge(ident_ready, 1)
            step(0)
            with pe.Fori(0, BLOCKS - 1) as b:
                step(BLOCK_STEPS * b + 1)
                step(BLOCK_STEPS * b + 2, mlp_stages(b, BLOCK * b, 2 * BLOCK_STEPS * (b + 1)))
            step(STEPS - 1)
            for _, stage in sorted(mlp_stages(BLOCKS - 1, BATCH - BLOCK, 2 * STEPS).items()):
                stage()

        @block.vector
        def _(dve):
            dve.wait_ge(ids_loaded, 16)
            nc.vector.transpose(ids_t[:], ids_in[:]).then_inc(ids_turned, 1)
            dve.wait_ge(ids_turned, 1)
            dve.wait_ge(base_loaded, 16)
            nc.vector.tensor_tensor(idx[:], ids_t[:], base_sb[:, 0:1].to_broadcast([P, GROUPS]),
                                    ALU.add).then_inc(idx_ready, 1)
            dve.sem_inc(z_dve, 2)
            dve.sem_inc(y_free, 1)
            def copy_pair(s, p):
                dve.wait_ge(transposed, STEP * s + 2 * p + 2)
                nc.vector.tensor_copy(xt[:, 0], xt_ps[:, 0]).then_inc(xt_dve, 1)

            def dots(s, slot0, count):
                dve.wait_ge(gram_done, PAIRS * s + (slot0 + count) // 2)
                return copy_dots(nc.vector.tensor_copy, (0, 1), STEP * s + slot0, slot0, count)

            def step(s, mlp=None, first=False, last=False):
                for p in range(0, PAIRS, 2):
                    copy_pair(s, p)
                    if p == 0 and not first:
                        dots(s - 1, HALF, HALF).then_inc(z_dve, 1)
                    if last and p == PAIRS - 2:
                        dots(s, HALF, HALF // 2)
                    if mlp and p in mlp:
                        mlp[p]()
                    if p == PAIRS // 2:
                        dots(s, 0, HALF).then_inc(z_dve, 1)
                if last:
                    dots(s, HALF + HALF // 2, HALF // 2).then_inc(z_dve, 1)

            def h1_relu(b):
                dve.wait_ge(h1_done, 2 * b + 2)
                for m in (2, 3):
                    last = nc.vector.tensor_scalar(h1[:, m, :], mlp_ps[:, 1, m % 2, :],
                                                   b1[:, m:m + 1], 0.0, ALU.add, ALU.max)
                last.then_inc(h1_dve, 1)

            def h2_relu(b):
                dve.wait_ge(h2_done, 2 * b + 2)
                nc.vector.tensor_scalar(h2[:, 1, :], mlp_ps[:, 1, 2, :], b2[:, 1:2], 0.0,
                                        ALU.add, ALU.max).then_inc(h2_dve, 1)

            def y_copy(b):
                dve.wait_ge(y_done, b + 1)
                nc.vector.tensor_copy(
                    y_by_column[:, bass.ds(b, 1), :, :],
                    y_ps.rearrange("o (c r q) -> o c r q", c=1, q=QUADS)).then_inc(y_free, 1)

            def mlp_stages(b):
                def tail():
                    h2_relu(b)
                    y_copy(b)

                return {4: lambda: h1_relu(b), 6: tail}

            step(0, first=True)
            dve.wait_ge(dense_loaded, 16)
            nc.vector.transpose(dense_t[:], dense_in[:]).then_inc(dense_turned, 1)
            dve.wait_ge(dense_turned, 1)
            for q in range(QUADS):
                last = nc.vector.tensor_copy(z_by_quad[0:FIELDS, q, :, 0],
                                             dense_t[FIELDS * q:FIELDS * (q + 1), :])
            last.then_inc(dense_ready, 1)
            dve.wait_ge(vec_loaded, 16)
            with dve.Fori(0, BLOCKS - 1) as b:
                step(BLOCK_STEPS * b + 1)
                step(BLOCK_STEPS * b + 2, mlp_stages(b))
            step(STEPS - 1, last=True)
            for _, stage in sorted(mlp_stages(BLOCKS - 1).items()):
                stage()

        @block.scalar
        def _(act):
            act.dma_start(base_sb[:], row_base).then_inc(base_loaded, 16)
            act.dma_start(vec_sb[:], vectors).then_inc(vec_loaded, 16)
            act.sem_inc(z_act, 2)

            def copy_pair(s, p):
                act.wait_ge(transposed, STEP * s + 2 * p + 2)
                nc.scalar.copy(xt[:, 1], xt_ps[:, 1]).then_inc(xt_act, 1)

            def dots(s, slot0, count):
                act.wait_ge(gram_done, PAIRS * s + (slot0 + count) // 2)
                return copy_dots(nc.scalar.copy, (2, 3), STEP * s + slot0, slot0, count)

            def step(s, mlp=None, first=False, last=False):
                for p in range(1, PAIRS, 2):
                    copy_pair(s, p)
                    if p == 1 and not first:
                        dots(s - 1, HALF, HALF).then_inc(z_act, 1)
                    if mlp and p in mlp:
                        mlp[p]()
                    if p == PAIRS // 2 - 1:
                        dots(s, 0, HALF).then_inc(z_act, 1)
                if last:
                    dots(s, HALF, HALF // 2)
                    dots(s, HALF + HALF // 2, HALF // 2).then_inc(z_act, 1)

            def h1_relu(b):
                act.wait_ge(h1_done, 2 * b + 1)
                for m in (0, 1):
                    last = nc.scalar.activation(h1[:, m, :], mlp_ps[:, 0, m, :], ACT.Relu,
                                                bias=b1[:, m:m + 1])
                last.then_inc(h1_act, 1)

            def h2_relu(b):
                act.wait_ge(h2_done, 2 * b + 1)
                nc.scalar.activation(h2[:, 0, :], mlp_ps[:, 0, 2, :], ACT.Relu,
                                     bias=b2[:, 0:1]).then_inc(h2_act, 1)

            def mlp_stages(b):
                return {3: lambda: h1_relu(b), 5: lambda: h2_relu(b)}

            step(0, first=True)
            act.wait_ge(vec_loaded, 16)
            with act.Fori(0, BLOCKS - 1) as b:
                step(BLOCK_STEPS * b + 1)
                step(BLOCK_STEPS * b + 2, mlp_stages(b))
            step(STEPS - 1, last=True)
            for _, stage in sorted(mlp_stages(BLOCKS - 1).items()):
                stage()


def interaction_weights(w_top1):
    import numpy as np

    out = np.zeros((QUADS, FIELDS, SLOTS, w_top1.shape[1]), w_top1.dtype)
    i, j = np.triu_indices(FIELDS, k=1)
    out[j // SLOTS, i, j % SLOTS] = w_top1[:len(i)]
    out[0, :DENSE, 0] = w_top1[len(i):]
    return out.reshape(P, SLOTS, -1)


def kernel(**inputs):
    import numpy as np
    import concourse.bacc as bacc
    from concourse.bass_utils import run_bass_kernel_spmd

    a = {name: np.asarray(x) for name, x in inputs.items()}
    tables = [a[f"tbl_{f}"] for f in range(FIELDS)]
    starts = np.cumsum([0] + [len(t) for t in tables[:-1]]).astype(np.int32)
    dense = np.zeros((BATCH, FIELDS), a["dense_ctx"].dtype)
    dense[:, :DENSE] = a["dense_ctx"]
    arrays = {
        "ids": np.ascontiguousarray(a["ids"]),
        "row_base": np.tile(starts, QUADS).reshape(P, 1),
        "tables": np.concatenate(tables, axis=0),
        "dense": dense,
        "w1": interaction_weights(a["W_top1"]),
        "w2": np.ascontiguousarray(a["W_top2"]),
        "vectors": np.ascontiguousarray(np.concatenate(
            [a[n].reshape(-1, P) for n in ("b_top1", "b_top2", "W_top3")], axis=0).T),
    }
    nc = bacc.Bacc("TRN2", target_bir_lowering=False, num_devices=1)
    args = [nc.dram_tensor(name, x.shape, mybir.dt.from_np(x.dtype), kind="ExternalInput").ap()
            for name, x in arrays.items()]
    y = nc.dram_tensor("y", (BATCH, 1), F32, kind="ExternalOutput").ap()
    tower_kernel(nc, *args, y)
    run = run_bass_kernel_spmd(nc, [arrays], core_ids=[0])
    return run.results[0]["y"]
```

```python
from contextlib import ExitStack

import concourse.bass as bass
from concourse import mybir

F32 = mybir.dt.float32
I32 = mybir.dt.int32
ALU = mybir.AluOpType
ACT = mybir.ActivationFunctionType

P = 128
FIELDS = 32
QUADS = P // FIELDS
BATCH = 512
DIM = 256
CHUNKS = DIM // P
GROUPS = BATCH // QUADS
STEP = 16
PAIRS = STEP // 2
HALF = STEP // 2
STEPS = GROUPS // STEP
BLOCK_STEPS = 2
BLOCK = BLOCK_STEPS * STEP * QUADS
BLOCKS = BATCH // BLOCK
SLOTS = FIELDS // QUADS
H1 = 512
H2 = 256
N1 = H1 // P
N2 = H2 // P
DENSE = 16


def tower_kernel(nc, ids, tables, dense, w1, w2, vectors, y):
    with ExitStack() as ctx:
        def sb(name, shape, dt=F32):
            return ctx.enter_context(nc.sbuf_tensor(name, shape, dt))

        def psum(name, shape):
            return ctx.enter_context(nc.psum_tensor(name, shape, F32))

        def sem(name):
            return ctx.enter_context(nc.semaphore(name))

        ids_sb = sb("ids_sb", [P, GROUPS + 1], I32)
        idx = sb("idx", [P, GROUPS], I32)
        ident = sb("ident", [P, P])
        rows = sb("rows", [P, STEP, DIM])
        xt = sb("xt", [P, 2, 2, DIM])
        z = sb("z", [P, SLOTS, BATCH])
        w1_sb = sb("w1_sb", [P, SLOTS, H1])
        w2_sb = sb("w2_sb", [P, N1, H2])
        vec_sb = sb("vec_sb", [P, N1 + 2 * N2])
        h1 = sb("h1", [P, N1, BLOCK])
        h2 = sb("h2", [P, N2, BLOCK])
        y_row = sb("y_row", [1, BATCH])
        b1 = vec_sb[:, 0:N1]
        b2 = vec_sb[:, N1:N1 + N2]
        w3 = vec_sb[:, N1 + N2:N1 + 2 * N2]

        xt_ps = psum("xt_ps", [P, 2, 2, DIM])
        gram_ps = psum("gram_ps", [P, 2, HALF, P])
        act_ps = psum("act_ps", [P, 4, BLOCK])
        dve_ps = psum("dve_ps", [P, 2, BLOCK])
        h1_ps = [act_ps[:, 0, :], act_ps[:, 1, :], act_ps[:, 2, :], dve_ps[:, 0, :]]
        h2_ps = [act_ps[:, 3, :], dve_ps[:, 1, :]]
        y_ps = act_ps[0:1, 0, :]

        ids_loaded = sem("ids_loaded")
        dense_loaded = sem("dense_loaded")
        w1_loaded = sem("w1_loaded")
        w2_loaded = sem("w2_loaded")
        vec_loaded = sem("vec_loaded")
        idx_ready = sem("idx_ready")
        ident_zeroed = sem("ident_zeroed")
        ident_ready = sem("ident_ready")
        rows_landed = [sem(f"rows_landed_{n}") for n in range(STEP)]
        transposed = sem("transposed")
        xt_dve = sem("xt_dve")
        xt_act = sem("xt_act")
        gram_done = sem("gram_done")
        z_dve = sem("z_dve")
        z_act = sem("z_act")
        h1_done = sem("h1_done")
        h1_act = sem("h1_act")
        h1_dve = sem("h1_dve")
        h2_done = sem("h2_done")
        h2_act = sem("h2_act")
        h2_dve = sem("h2_dve")
        y_done = sem("y_done")
        y_free = sem("y_free")
        y_stored = sem("y_stored")

        z_by_quad = z[:].rearrange("p s (g q) -> p q g s", q=QUADS)

        def copy_dots(copy, quads, first, slot0, count):
            half, at = slot0 // HALF, slot0 % HALF
            for q in quads:
                for jq in range(QUADS):
                    lo = 1 if jq == 0 else 0
                    j0 = FIELDS * q + SLOTS * jq
                    last = copy(
                        z_by_quad[FIELDS * jq:FIELDS * (jq + 1), q, bass.ds(first, count), lo:SLOTS],
                        gram_ps[FIELDS * q:FIELDS * (q + 1), half, at:at + count, j0 + lo:j0 + SLOTS])
            return last

        block = ctx.enter_context(nc.Block())

        @block.sync
        def _(sp):
            sp.dma_start(ids_sb[:], ids).then_inc(ids_loaded, 16)
            sp.wait_ge(transposed, 2)
            sp.dma_start(z[0:FIELDS, 0, :], dense).then_inc(dense_loaded, 16)
            for n in range(SLOTS):
                sp.wait_ge(transposed, n + 3)
                sp.dma_start(w1_sb[:, n, :], w1[:, n, :]).then_inc(w1_loaded, 16)
            sp.wait_ge(transposed, SLOTS + 3)
            sp.dma_start(w2_sb[:], w2.rearrange("(k p) n -> p k n", p=P)).then_inc(w2_loaded, 16)
            sp.wait_ge(y_free, 1 + BLOCKS)
            sp.dma_start(y.rearrange("b o -> o b"), y_row[:]).then_inc(y_stored, 16)
            sp.wait_ge(y_stored, 16)

        @block.gpsimd
        def _(pool):
            nc.gpsimd.memset(ident[:], 0.0).then_inc(ident_zeroed, 1)
            pool.wait_ge(ident_zeroed, 1)
            nc.gpsimd.affine_select(out=ident[:], in_=ident[:], compare_op=ALU.not_equal, fill=1.0,
                                    base=0, pattern=[[-1, P]], channel_multiplier=1).then_inc(ident_ready, 1)
            pool.wait_ge(idx_ready, 1)
            for g in range(GROUPS):
                if g == STEP:
                    pool.wait_ge(idx_ready, 2)
                if g >= STEP:
                    pool.wait_ge(transposed, g - STEP + 1)
                pool.indirect_dma_start(rows[:, g % STEP, :], None, tables,
                                        bass.IndirectOffsetOnAxis(idx[:, g:g + 1], 0)
                                        ).then_inc(rows_landed[g % STEP], 16)

        @block.tensor
        def _(pe):
            def transpose_group(s, n, bank, place):
                pe.wait_ge(rows_landed[n], 16 * (s + 1))
                for k in range(CHUNKS):
                    last = nc.tensor.transpose(xt_ps[:, bank, place, P * k:P * (k + 1)],
                                               rows[:, n, P * k:P * (k + 1)], ident[:])
                last.then_inc(transposed, 1)

            def gram_group(n, bank, place):
                for k in range(CHUNKS):
                    x = xt[:, bank, place, P * k:P * (k + 1)]
                    last = nc.tensor.matmul(gram_ps[:, n // HALF, n % HALF, :], x, x,
                                            start=(k == 0), stop=(k == CHUNKS - 1))
                return last

            def transpose_pair(s, p):
                for place in range(2):
                    transpose_group(s, 2 * p + place, p % 2, place)

            def gram_pair(s, p):
                if p % (HALF // 2) == 0:
                    pe.wait_ge(z_dve, 2 * s + 2 * p // HALF + 1)
                    pe.wait_ge(z_act, 2 * s + 2 * p // HALF + 1)
                pe.wait_ge(xt_act if p % 2 else xt_dve, PAIRS // 2 * s + p // 2 + 1)
                gram_group(2 * p, p % 2, 0)
                gram_group(2 * p + 1, p % 2, 1).then_inc(gram_done, 1)

            def step(s, mlp=None, last=False):
                for p in range(1, PAIRS - last):
                    transpose_pair(s, p)
                    gram_pair(s, p - 1)
                    if mlp and p in mlp:
                        mlp[p]()
                if not last:
                    transpose_pair(s + 1, 0)
                    gram_pair(s, PAIRS - 1)
                    return
                transpose_group(s, STEP - 2, 1, 0)
                gram_pair(s, PAIRS - 2)
                transpose_group(s, STEP - 1, 0, 0)
                pe.wait_ge(xt_act, PAIRS // 2 * (s + 1))
                gram_group(STEP - 2, 1, 0)
                pe.wait_ge(xt_dve, PAIRS // 2 * (s + 1) + 1)
                gram_group(STEP - 1, 0, 0).then_inc(gram_done, 1)

            def h1_part(col, features):
                for m in features:
                    for s in range(SLOTS):
                        last = nc.tensor.matmul(h1_ps[m], w1_sb[:, s, P * m:P * (m + 1)],
                                                z[:, s, bass.ds(col, BLOCK)],
                                                start=(s == 0), stop=(s == SLOTS - 1))
                last.then_inc(h1_done, 1)

            def h2_all(b):
                for m in range(N2):
                    for k in range(N1):
                        if m == 0 and k in (0, N1 - 1):
                            pe.wait_ge(h1_dve if k else h1_act, b + 1)
                        last = nc.tensor.matmul(h2_ps[m], w2_sb[:, k, P * m:P * (m + 1)],
                                                h1[:, k, :], start=(k == 0), stop=(k == N1 - 1))
                    last.then_inc(h2_done, 1)

            def y_all(b):
                for m in range(N2):
                    pe.wait_ge(h2_dve if m else h2_act, b + 1)
                    last = nc.tensor.matmul(y_ps[:, :], w3[:, m:m + 1], h2[:, m, :],
                                            start=(m == 0), stop=(m == N2 - 1))
                last.then_inc(y_done, 1)

            def mlp_stages(b, col, halves):
                def first():
                    pe.wait_ge(z_dve, 2 + halves)
                    pe.wait_ge(z_act, 2 + halves)
                    pe.wait_ge(y_free, b + 1)
                    h1_part(col, range(N1 - 1))

                return {1: first, 2: lambda: h1_part(col, [N1 - 1]),
                        4: lambda: h2_all(b), 5: lambda: y_all(b)}

            pe.wait_ge(ident_ready, 1)
            transpose_pair(0, 0)
            step(0)
            pe.wait_ge(dense_loaded, 16)
            pe.wait_ge(w1_loaded, 16 * SLOTS)
            pe.wait_ge(w2_loaded, 16)
            pe.wait_ge(vec_loaded, 16)
            with pe.Fori(0, BLOCKS - 1) as b:
                step(BLOCK_STEPS * b + 1)
                step(BLOCK_STEPS * b + 2, mlp_stages(b, BLOCK * b, 2 * BLOCK_STEPS * (b + 1)))
            step(STEPS - 1, last=True)
            for _, stage in sorted(mlp_stages(BLOCKS - 1, BATCH - BLOCK, 2 * STEPS).items()):
                stage()

        @block.vector
        def _(dve):
            dve.wait_ge(ids_loaded, 16)
            for lo, hi in ((0, STEP), (STEP, GROUPS)):
                nc.vector.tensor_tensor(idx[:, lo:hi], ids_sb[:, lo:hi],
                                        ids_sb[:, GROUPS:GROUPS + 1].to_broadcast([P, hi - lo]),
                                        ALU.add).then_inc(idx_ready, 1)
            dve.sem_inc(z_dve, 2)
            dve.sem_inc(y_free, 1)

            def copy_pair(s, p):
                dve.wait_ge(transposed, STEP * s + 2 * p + 2)
                nc.vector.tensor_copy(xt[:, 0], xt_ps[:, 0]).then_inc(xt_dve, 1)

            def dots(s, slot0, count):
                dve.wait_ge(gram_done, PAIRS * s + (slot0 + count) // 2)
                return copy_dots(nc.vector.tensor_copy, (0, 1), STEP * s + slot0, slot0, count)

            def step(s, mlp=None, last=False):
                for p in range(2, PAIRS, 2):
                    copy_pair(s, p)
                    if mlp:
                        mlp[p]()
                    if p == PAIRS // 2:
                        dots(s, 0, HALF).then_inc(z_dve, 1)
                if not last:
                    copy_pair(s + 1, 0)
                    dots(s, HALF, HALF).then_inc(z_dve, 1)
                    return
                dots(s, HALF, HALF // 2)
                dve.wait_ge(transposed, STEP * (s + 1))
                nc.vector.tensor_copy(xt[:, 0, 0], xt_ps[:, 0, 0]).then_inc(xt_dve, 1)
                dots(s, HALF + HALF // 2, HALF // 2).then_inc(z_dve, 1)

            def h1_relu(b):
                m = N1 - 1
                dve.wait_ge(h1_done, 2 * b + 2)
                nc.vector.tensor_scalar(h1[:, m, :], h1_ps[m], b1[:, m:m + 1], 0.0,
                                        ALU.add, ALU.max).then_inc(h1_dve, 1)

            def h2_relu(b):
                dve.wait_ge(h2_done, 2 * b + 2)
                nc.vector.tensor_scalar(h2[:, 1, :], h2_ps[1], b2[:, 1:2], 0.0,
                                        ALU.add, ALU.max).then_inc(h2_dve, 1)

            def y_copy(b):
                dve.wait_ge(y_done, b + 1)
                nc.vector.tensor_copy(y_row[:, bass.ts(b, BLOCK)], y_ps).then_inc(y_free, 1)

            def mlp_stages(b):
                return {2: lambda: h1_relu(b), 4: lambda: h2_relu(b), 6: lambda: y_copy(b)}

            copy_pair(0, 0)
            step(0)
            dve.wait_ge(vec_loaded, 16)
            with dve.Fori(0, BLOCKS - 1) as b:
                step(BLOCK_STEPS * b + 1)
                step(BLOCK_STEPS * b + 2, mlp_stages(b))
            step(STEPS - 1, last=True)
            for _, stage in sorted(mlp_stages(BLOCKS - 1).items()):
                stage()

        @block.scalar
        def _(act):
            act.dma_start(vec_sb[:], vectors).then_inc(vec_loaded, 16)
            act.sem_inc(z_act, 2)

            def copy_pair(s, p):
                act.wait_ge(transposed, STEP * s + 2 * p + 2)
                nc.scalar.copy(xt[:, 1], xt_ps[:, 1]).then_inc(xt_act, 1)

            def dots(s, slot0, count):
                act.wait_ge(gram_done, PAIRS * s + (slot0 + count) // 2)
                return copy_dots(nc.scalar.copy, (2, 3), STEP * s + slot0, slot0, count)

            def step(s, mlp=None, last=False):
                for p in range(1, PAIRS - last, 2):
                    copy_pair(s, p)
                    if p == PAIRS // 2 - 1:
                        dots(s, 0, HALF).then_inc(z_act, 1)
                    if mlp and p in mlp:
                        mlp[p]()
                if not last:
                    dots(s, HALF, HALF).then_inc(z_act, 1)
                    return
                dots(s, HALF, HALF // 2)
                act.wait_ge(transposed, STEP * (s + 1) - 1)
                nc.scalar.copy(xt[:, 1, 0], xt_ps[:, 1, 0]).then_inc(xt_act, 1)
                dots(s, HALF + HALF // 2, HALF // 2).then_inc(z_act, 1)

            def h1_relu(b):
                act.wait_ge(h1_done, 2 * b + 1)
                for m in range(N1 - 1):
                    last = nc.scalar.activation(h1[:, m, :], h1_ps[m], ACT.Relu,
                                                bias=b1[:, m:m + 1])
                last.then_inc(h1_act, 1)

            def h2_relu(b):
                act.wait_ge(h2_done, 2 * b + 1)
                nc.scalar.activation(h2[:, 0, :], h2_ps[0], ACT.Relu,
                                     bias=b2[:, 0:1]).then_inc(h2_act, 1)

            def mlp_stages(b):
                return {1: lambda: h1_relu(b), 3: lambda: h2_relu(b)}

            step(0)
            act.wait_ge(vec_loaded, 16)
            with act.Fori(0, BLOCKS - 1) as b:
                step(BLOCK_STEPS * b + 1)
                step(BLOCK_STEPS * b + 2, mlp_stages(b))
            step(STEPS - 1, last=True)
            for _, stage in sorted(mlp_stages(BLOCKS - 1).items()):
                stage()


def interaction_weights(w_top1):
    import numpy as np

    out = np.zeros((QUADS, FIELDS, SLOTS, w_top1.shape[1]), w_top1.dtype)
    i, j = np.triu_indices(FIELDS, k=1)
    out[j // SLOTS, i, j % SLOTS] = w_top1[:len(i)]
    out[0, :DENSE, 0] = w_top1[len(i):]
    return out.reshape(P, SLOTS, -1)


def kernel(**inputs):
    import numpy as np
    import concourse.bacc as bacc
    from concourse.bass_utils import run_bass_kernel_spmd

    a = {name: np.asarray(x) for name, x in inputs.items()}
    tables = [a[f"tbl_{f}"] for f in range(FIELDS)]
    starts = np.cumsum([0] + [len(t) for t in tables[:-1]]).astype(np.int32)
    ids = a["ids"].reshape(GROUPS, QUADS, FIELDS).transpose(1, 2, 0).reshape(P, GROUPS)
    dense = np.zeros((FIELDS, BATCH), a["dense_ctx"].dtype)
    dense[:DENSE] = a["dense_ctx"].T
    arrays = {
        "ids": np.concatenate([ids, np.tile(starts, QUADS).reshape(P, 1)], axis=1),
        "tables": np.concatenate(tables, axis=0),
        "dense": dense,
        "w1": interaction_weights(a["W_top1"]),
        "w2": np.ascontiguousarray(a["W_top2"]),
        "vectors": np.ascontiguousarray(np.concatenate(
            [a[n].reshape(-1, P) for n in ("b_top1", "b_top2", "W_top3")], axis=0).T),
    }
    nc = bacc.Bacc("TRN2", target_bir_lowering=False, num_devices=1)
    args = [nc.dram_tensor(name, x.shape, mybir.dt.from_np(x.dtype), kind="ExternalInput").ap()
            for name, x in arrays.items()]
    y = nc.dram_tensor("y", (BATCH, 1), F32, kind="ExternalOutput").ap()
    tower_kernel(nc, *args, y)
    run = run_bass_kernel_spmd(nc, [arrays], core_ids=[0])
    return run.results[0]["y"]
```
